# Optimizing a Trainium2 kernel written in Bass

```python
import numpy as np
import jax
import jax.numpy as jnp

def _softmax(x, axis=-1):
    return jax.nn.softmax(x, axis=axis)

def _gelu(x):
    return jax.nn.gelu(x, approximate=True)

def _silu(x):
    return jax.nn.silu(x)

def _sigmoid(x):
    return jax.nn.sigmoid(x)

def _layernorm(x, axis=-1, eps=1e-05):
    m = jnp.mean(x, axis=axis, keepdims=True)
    v = jnp.var(x, axis=axis, keepdims=True)
    return (x - m) / jnp.sqrt(v + eps)

def _scatter_add(tgt, idx, src, axis=0):
    return tgt.at[idx].add(src)

def _segment_sum(src, seg, n):
    return jax.ops.segment_sum(src, seg, n)
kernel_name = 'mk_gnn_resnorm_d2_gnn_r8_f82121'

def setup_inputs(seed: int=0):
    np.random.seed(seed)
    _w = jnp.asarray

    def _rec_inputs():
        import jax
        import jax.numpy as jnp
        _gk = jax.random.key(seed)
        x = -0.0005121 + 1.001 * jax.random.normal(jax.random.fold_in(_gk, 1), (12500, 64), jnp.float32)
        src = jax.random.randint(jax.random.fold_in(_gk, 2), (200000,), 0, 12500, jnp.int32)
        dst = jnp.minimum((12500 * jax.random.uniform(jax.random.fold_in(_gk, 3), (200000,)) ** 2.0).astype(jnp.int32), 99999)
        _o = jnp.argsort(dst, stable=True)
        src = src[_o]
        dst = dst[_o]
        edge_attr_64 = -9.77346e-05 + 0.999888 * jax.random.normal(jax.random.fold_in(_gk, 12), (200000, 64), jnp.float32)
        return (x, src, dst, edge_attr_64)
    x, src, dst, edge_attr_64 = _rec_inputs()

    def _L0_gnn_setup():
        import jax, jax.numpy as jnp
        import numpy as np
        N_NODES = 6250
        N_EDGES = 100000
        D = 64
        H = 128
        key = jax.random.key(seed)
        ks = jax.random.split(key, 8)
        s = 0.05
        return {'nodes': jax.random.normal(ks[0], (N_NODES, D), jnp.float32), 'edges': jax.random.normal(ks[1], (N_EDGES, D), jnp.float32), 'We1': jax.random.normal(ks[2], (3 * D, H), jnp.float32) * s, 'be1': jnp.zeros((H,), jnp.float32), 'We2': jax.random.normal(ks[3], (H, D), jnp.float32) * s, 'be2': jnp.zeros((D,), jnp.float32), 'Wn1': jax.random.normal(ks[4], (2 * D, H), jnp.float32) * s, 'bn1': jnp.zeros((H,), jnp.float32), 'Wn2': jax.random.normal(ks[5], (H, D), jnp.float32) * s, 'bn2': jnp.zeros((D,), jnp.float32), 'senders': jax.random.randint(ks[6], (N_EDGES,), 0, N_NODES, jnp.int32), 'receivers': jax.random.randint(ks[7], (N_EDGES,), 0, N_NODES, jnp.int32)}
    _L0_gnn_all = _L0_gnn_setup()
    _L0_gnn_in = {k: v for k, v in _L0_gnn_all.items() if k in ('We1', 'be1', 'We2', 'be2', 'Wn1', 'bn1', 'Wn2', 'bn2')}
    del _L0_gnn_all

    def _L1_gnn_setup():
        import jax, jax.numpy as jnp
        import numpy as np
        N_NODES = 12500
        N_EDGES = 200000
        IN_CH = 64
        OUT_CH = 64
        key = jax.random.key(seed)
        ks = jax.random.split(key, 6)
        x = jax.random.normal(ks[0], (N_NODES, IN_CH), dtype=jnp.float32)
        edge_index = jax.random.randint(ks[1], (2, N_EDGES), 0, N_NODES, dtype=jnp.int64)
        W1 = jax.random.normal(ks[2], (2 * IN_CH, OUT_CH), dtype=jnp.float32) * (1.0 / np.sqrt(2 * IN_CH))
        b1 = jnp.zeros((OUT_CH,), dtype=jnp.float32)
        W2 = jax.random.normal(ks[3], (OUT_CH, OUT_CH), dtype=jnp.float32) * (1.0 / np.sqrt(OUT_CH))
        b2 = jnp.zeros((OUT_CH,), dtype=jnp.float32)
        return {'x': x, 'edge_index': edge_index, 'W1': W1, 'b1': b1, 'W2': W2, 'b2': b2}
    _L1_gnn_all = _L1_gnn_setup()
    _L1_gnn_in = {k: v for k, v in _L1_gnn_all.items() if k in ('W1', 'b1', 'W2', 'b2')}
    del _L1_gnn_all
    return {'x': x, 'src': src, 'dst': dst, 'edge_attr_64': edge_attr_64, 'L0_gnn_We1': _L0_gnn_in['We1'], 'L0_gnn_be1': _L0_gnn_in['be1'], 'L0_gnn_We2': _L0_gnn_in['We2'], 'L0_gnn_be2': _L0_gnn_in['be2'], 'L0_gnn_Wn1': _L0_gnn_in['Wn1'], 'L0_gnn_bn1': _L0_gnn_in['bn1'], 'L0_gnn_Wn2': _L0_gnn_in['Wn2'], 'L0_gnn_bn2': _L0_gnn_in['bn2'], 'L1_gnn_W1': _L1_gnn_in['W1'], 'L1_gnn_b1': _L1_gnn_in['b1'], 'L1_gnn_W2': _L1_gnn_in['W2'], 'L1_gnn_b2': _L1_gnn_in['b2']}

def reference(x, src, dst, edge_attr_64, L0_gnn_We1, L0_gnn_be1, L0_gnn_We2, L0_gnn_be2, L0_gnn_Wn1, L0_gnn_bn1, L0_gnn_Wn2, L0_gnn_bn2, L1_gnn_W1, L1_gnn_b1, L1_gnn_W2, L1_gnn_b2):
    import jax
    import jax.numpy as jnp

    def _L0_gnn_ref(nodes, edges, We1, be1, We2, be2, Wn1, bn1, Wn2, bn2, senders, receivers):
        import jax, jax.numpy as jnp
        import numpy as np
        N_NODES = 6250
        N_EDGES = 100000
        D = 64
        H = 128
        edge_in = jnp.concatenate([edges, nodes[receivers], nodes[senders]], axis=-1)
        h = jax.nn.relu(edge_in @ We1 + be1)
        new_edges = h @ We2 + be2
        agg = jax.ops.segment_sum(new_edges, receivers, num_segments=nodes.shape[0])
        node_in = jnp.concatenate([agg, nodes], axis=-1)
        h2 = jax.nn.relu(node_in @ Wn1 + bn1)
        new_nodes = h2 @ Wn2 + bn2
        return new_nodes

    def _L1_gnn_ref(x, edge_index, W1, b1, W2, b2):
        import jax, jax.numpy as jnp
        import numpy as np
        N_NODES = 12500
        N_EDGES = 200000
        IN_CH = 64
        OUT_CH = 64
        src = edge_index[0]
        dst = edge_index[1]
        x_i = x[dst]
        x_j = x[src]
        edge_features = jnp.concatenate([x_i, x_j - x_i], axis=-1)
        h = jax.nn.relu(edge_features @ W1 + b1)
        edge_messages = h @ W2 + b2
        out = jax.ops.segment_max(edge_messages, dst, num_segments=x.shape[0])
        return jnp.where(jnp.isfinite(out), out, jnp.zeros_like(out))
    edge_index = jnp.stack([src, dst])
    x = _layernorm(x + _L0_gnn_ref(x, edge_attr_64, L0_gnn_We1, L0_gnn_be1, L0_gnn_We2, L0_gnn_be2, L0_gnn_Wn1, L0_gnn_bn1, L0_gnn_Wn2, L0_gnn_bn2, src, dst), axis=-1)
    x = _layernorm(x + _L1_gnn_ref(x, edge_index, L1_gnn_W1, L1_gnn_b1, L1_gnn_W2, L1_gnn_b2), axis=-1)
    return x

_drawn_inputs = setup_inputs


def setup_inputs(seed=0):
    import zlib

    import numpy as np

    out = dict(_drawn_inputs(seed))
    spreads = {'L0_gnn_be1': (0.0, 0.1),
     'L0_gnn_be2': (0.0, 0.1),
     'L0_gnn_bn1': (0.0, 0.1),
     'L0_gnn_bn2': (0.0, 0.1),
     'L1_gnn_b1': (0.0, 0.1),
     'L1_gnn_b2': (0.0, 0.1)}
    factors = {}
    for name, (base, spread) in spreads.items():
        noise = np.random.default_rng([zlib.crc32(name.encode()), seed]).standard_normal(out[name].shape)
        drawn = base * np.exp(spread * noise) if base else spread * noise
        out[name] = jnp.asarray(drawn.astype(out[name].dtype))
    for name, factor in factors.items():
        out[name] = (out[name] * factor).astype(out[name].dtype)
    return out
```

```python
import concourse.bass as bass
from concourse import mybir
from contextlib import ExitStack

F32 = mybir.dt.float32
BF16 = mybir.dt.bfloat16
I32 = mybir.dt.int32
U32 = mybir.dt.uint32
ALU = mybir.AluOpType
ACT = mybir.ActivationFunctionType
AX = mybir.AxisListType

P = 128
D = 64
H = 128
RING = 4
TILES = 4
GROUP = TILES * P
BODY = RING * GROUP
EROW = 512
VCOL = 4
CCOL = 7
BIG = 3.0e38
EPS = 1e-5


def sizes(n_nodes, n_edges):
    cols = -(-n_nodes // P)
    cols = -(-cols // (2 * CCOL)) * 2 * CCOL
    iters = -(-(n_edges + P) // BODY)
    return cols, iters


class Step:

    def __init__(self, ring, it, off):
        self.n = it * ring + off
        self.slot = off % ring
        self.pair = off % 2
        self.turn = it + off // ring


def run_pipeline(eng, ring, count, stages, first=0):
    deepest = max(lag for lag, _ in stages)
    peel = -(-(deepest + ring) // ring)

    def peeled(s):
        for lag, f in stages:
            if first <= s - lag < count:
                f(Step(ring, 0, s - lag))

    for s in range(peel * ring):
        peeled(s)
    with eng.Fori(peel, count // ring) as it:
        for j in range(ring):
            for lag, f in stages:
                f(Step(ring, it, j - lag))
    for s in range(count, count + deepest):
        peeled(s)


def build(nc, ins, out):
    x_rows, x_cols, src_idx, dst_ext, dst_last, edges_t = (
        ins[k] for k in ("x_rows", "x_cols", "src_idx", "dst_ext", "dst_last", "edges_t"))
    COLS = x_cols.shape[1] // P
    NODES = COLS * P
    ITERS = edges_t.shape[1] // BODY
    EDGES = ITERS * BODY
    GROUPS = ITERS * RING
    ETILES = GROUPS * TILES
    BTILES = RING * TILES
    CHUNKS = COLS // CCOL
    CW = CCOL * P
    EROWS = EDGES // EROW
    RANKS = NODES + P
    SKIP = 2 * RANKS
    assert ITERS <= P and CHUNKS % 2 == 0

    with ExitStack() as ctx:
        def sb(name, shape, dt=F32):
            return ctx.enter_context(nc.sbuf_tensor(name, shape, dt))

        def sem(name):
            return ctx.enter_context(nc.semaphore(name))

        def dram(name, shape, dt=F32):
            return nc.dram_tensor(name, shape, dt, kind="Internal").ap()

        rank_tab = [dram("rank_tab0", (RANKS, H)), dram("rank_tab1", (RANKS, D))]
        src_tab1 = dram("src_tab1", (NODES, D))
        edge_rows = [dram("edge_rows0", (EDGES, D)), dram("edge_rows1", (EDGES, D))]
        dst_f = dram("dst_f", (EROWS, EROW))
        base_d = dram("base_d", (1, ETILES), I32)

        ps = ctx.enter_context(nc.psum_tensor("ps", [P, 8, 512], F32))

        ident = sb("ident", [P, P])
        ident_b = sb("ident_b", [P, P], BF16)
        tri = sb("tri", [P, P])
        shift = sb("shift", [P, P])
        part = sb("part", [P, 1])
        part_i = sb("part_i", [P, 1], I32)
        w_edge = sb("w_edge", [P, H])
        w_dst0 = sb("w_dst0", [D + 1, H])
        w_e2 = sb("w_e2", [H, D])
        w_n1 = sb("w_n1", [D, 2, H])
        w_n2 = sb("w_n2", [H, D])
        bn1 = sb("bn1", [H, 1])
        w_1 = sb("w_1", [D + 1, 2 * D])
        w_1a = sb("w_1a", [D + 1, D])
        w_2 = sb("w_2", [D, D])
        b2 = sb("b2", [D, 1])
        be2 = sb("be2", [P, D])
        bn2 = sb("bn2", [P, D])
        eps = sb("eps", [P, 1])
        zeros = sb("zeros", [P, H])

        xn = sb("xn", [P, COLS, D])
        xchunk = sb("xchunk", [D + 1, 2, CW])
        node = sb("node", [P, COLS])
        node_i = sb("node_i", [P, COLS], I32)
        node_h = sb("node_h", [P, COLS])
        signs = sb("signs", [P, COLS])
        cnt_row = sb("cnt_row", [P, COLS])
        cnt_in = sb("cnt_in", [P, COLS])
        cum = sb("cum", [P, COLS])
        deg = sb("deg", [P, COLS])
        has = sb("has", [P, COLS])
        lacks = sb("lacks", [P, COLS])
        rank = sb("rank", [P, COLS])
        rank_a = sb("rank_a", [P, COLS])
        rank_b = sb("rank_b", [P, COLS])
        end_idx = sb("end_idx", [P, COLS], I32)
        rank_idx = sb("rank_idx", [P, COLS], I32)
        gidx = sb("gidx", [P, 2, CCOL], I32)
        sidx = sb("sidx", [P, 2, CCOL], I32)
        pre_rows = sb("pre_rows", [P, 2, CCOL * H])

        esrc = sb("esrc", [P, ETILES + BTILES], I32)
        eidx = sb("eidx", [P, RING, TILES], I32)
        rows_in = sb("rows_in", [P, RING, TILES, D])
        RANK_IN_TILE, SAME, PENALTY = range(3)
        marks = sb("marks", [ITERS, 3, BODY], BF16)
        tile_base = sb("tile_base", [1, ETILES], I32)

        AREA = 20000
        area = sb("area", [P, AREA])

        def carve(spec):
            got, at = {}, 0
            for name, parts, shape, dt in spec:
                words = 1
                for s in shape:
                    words *= s
                v = area[0:parts, at:at + words]
                if dt != F32:
                    v = v.bitcast(dt)
                if len(shape) == 2:
                    v = v.rearrange("p (a b) -> p a b", a=shape[0])
                elif len(shape) == 3:
                    v = v.rearrange("p (a b c) -> p a b c", a=shape[0], b=shape[1])
                got[name] = v
                at += words
            assert at <= AREA, at
            return got

        prep = carve([("d0", ITERS, [BODY], I32), ("dm", ITERS, [BODY], I32), ("first", ITERS, [BODY], F32),
                      ("count", ITERS, [BODY], F32), ("df", ITERS, [BODY], F32),
                      ("base", ITERS, [BTILES], I32), ("last_i", P, [EROWS], I32),
                      ("last_f", P, [EROWS], F32), ("junk", P, [2, EROWS], F32), ("junk_s", P, [2, EROWS], F32),
                      ("rows", P, [2, CCOL, EROW], F32)])
        main = carve([("win", P, [RING, TILES, H], F32), ("stack", P, [RING, GROUP], F32),
                      ("onehot", P, [2, GROUP], F32), ("hid", P, [2, GROUP], F32),
                      ("scan", P, [RING, GROUP], F32), ("orow", P, [RING, TILES * D], F32),
                      ("msg", P, [2, GROUP], F32)])
        swp = carve([("got", P, [2, CCOL, D], F32), ("agg", P, [CCOL, D], F32),
                     ("tmp", P, [CCOL, D], F32), ("aggt", D, [CW], F32), ("h2", P, [CW], F32),
                     ("y", P, [CCOL, D], F32), ("cen", P, [CCOL, D], F32), ("sq", P, [CCOL, D], F32),
                     ("x1", P, [2, CCOL, D], F32), ("x1t", D + 1, [CW], F32),
                     ("bt", P, [2, CCOL, D], F32), ("at", P, [2, CCOL * D], F32),
                     ("sum", P, [CCOL], F32), ("var", P, [CCOL], F32), ("std", P, [CCOL], F32),
                     ("rstd", P, [CCOL], F32), ("ok", P, [CCOL, D], I32), ("res", P, [2, CCOL * D], F32)])

        s_w = sem("weights_in")
        s_first = sem("first_src_idx_in")
        s_src = sem("src_in")
        s_dst = sem("dst_in")
        s_last = sem("dst_row_ends_in")
        s_x = sem("x_in")
        s_const = sem("pool_constants_ready")
        s_zero = sem("zeros_ready")
        s_ones = sem("ones_rows_ready")
        s_fill = sem("rows_past_the_ranks_zeroed")
        s_dstf = sem("dst_floats_stored")
        s_small = sem("small_constants_ready")
        s_coarse = sem("columns_searched_by_rows")
        s_signs = sem("columns_searched_by_scalar")
        s_joined = sem("searched_columns_joined")
        s_sidx = sem("search_idx_ready")
        s_srow = [sem(f"search_rows_in{k}") for k in range(2)]
        s_counted = sem("search_rows_counted")
        s_np = sem("node_prep_steps")
        s_noff = sem("node_offsets_ready")
        s_ep = sem("edge_prep_steps")
        s_off = sem("edge_offsets_ready")
        s_base = sem("tile_bases_stored")
        s_base_in = sem("tile_bases_in")
        s_w1 = sem("layer1_weights_ready")
        s_xc = [sem(f"x_chunk_in{k}") for k in range(2)]
        s_ppre = sem("pre_products_done")
        s_pcopy = sem("pre_rows_ready")
        s_pscat = [sem(f"pre_rows_scattered{k}") for k in range(2)]
        s_carry = sem("first_carry_ready")

        def wait(eng, s, value):
            if isinstance(value, int) and value <= 0:
                return
            eng.wait_ge(s, value)

        def hold(eng, s, value):
            if isinstance(value, int) and value <= 0:
                return
            eng.wait_ge(s, value)
            eng.nop(nofuse=True)

        class Pass:

            def __init__(self, n):
                self.idx = sem(f"src_idx_ready_{n}")
                self.gathered = [sem(f"src_rows_in_{n}_{k}") for k in range(RING)]
                self.edges = [sem(f"edges_in_{n}_{k}") for k in range(RING)]
                self.windows = [sem(f"windows_in_{n}_{k}") for k in range(RING)]
                self.turned = sem(f"src_transposed_{n}")
                self.stacked = sem(f"src_stacked_{n}")
                self.ranks = sem(f"rank_spread_{n}")
                self.mask = sem(f"mask_spread_{n}")
                self.onehot = sem(f"onehot_ready_{n}")
                self.pre = sem(f"hidden_products_{n}")
                self.hid = sem(f"hidden_ready_{n}")
                self.msgp = sem(f"message_products_{n}")
                self.msg = sem(f"messages_ready_{n}")
                self.scan = sem(f"scan_done_{n}")
                self.rowsp = sem(f"edge_row_products_{n}")
                self.rows = sem(f"edge_rows_ready_{n}")
                self.stored = [sem(f"edge_rows_stored_{n}_{k}") for k in range(RING)]

        class Sweep:

            def __init__(self, n):
                self.idx = sem(f"end_idx_ready_{n}")
                self.got = [sem(f"end_rows_in_{n}_{k}") for k in range(2)]
                self.x = [sem(f"sweep_x_chunk_in_{n}_{k}") for k in range(2)]
                self.a = sem(f"sweep_agg_steps_{n}")
                self.v = sem(f"sweep_norm_steps_{n}")
                self.agg = sem(f"agg_ready_{n}")
                self.aggp = sem(f"agg_transposed_{n}")
                self.aggt = sem(f"aggt_ready_{n}")
                self.h2p = sem(f"node_hidden_products_{n}")
                self.h2 = sem(f"node_hidden_ready_{n}")
                self.newp = sem(f"node_products_{n}")
                self.newr = sem(f"node_products_read_{n}")
                self.copied = sem(f"x1_copied_{n}")
                self.var = sem(f"variance_ready_{n}")
                self.std = sem(f"deviation_ready_{n}")
                self.rstd = sem(f"inverse_deviation_ready_{n}")
                self.x1 = sem(f"normed_ready_{n}")
                self.x1p = sem(f"normed_transposed_{n}")
                self.x1t = sem(f"normed_t_ready_{n}")
                self.tabp = sem(f"table_products_{n}")
                self.tab = sem(f"tables_ready_{n}")
                self.kept = sem(f"normed_kept_{n}")
                self.stored = [sem(f"sweep_rows_stored_{n}_{k}") for k in range(2)]
                self.scattered = [sem(f"rank_rows_scattered_{n}_{k}") for k in range(2)]

        passes = [Pass(0), Pass(1)]
        sweeps = [Sweep(0), Sweep(1)]
        AGG_LAG, X1T_LAG = 1, 4
        LINKS = (3, 5)
        HALVES = ((0, 4), (4, CCOL))
        CHUNK_DMAS = 16 * CCOL

        def chunk_cols(c):
            return bass.ds(c.n * CCOL, CCOL)

        block = ctx.enter_context(nc.Block())

        @block.sync
        def _(sp):
            sp.dma_start(eidx[:, :, :].rearrange("p a b -> p (a b)"), src_idx[:, 0:BTILES]).then_inc(s_first, 16)
            sp.dma_start(prep["d0"], dst_ext[0, 1:1 + EDGES].rearrange("(p w) -> p w", p=ITERS)).then_inc(s_dst, 16)
            sp.dma_start(prep["last_i"], dst_last.partition_broadcast(P)).then_inc(s_last, 16)
            sp.dma_start(esrc[:, :], src_idx).then_inc(s_src, 16)
            we1, w1 = ins["We1"], ins["W1"]
            for dst, src in (
                    (w_dst0[0:D, :], we1[D:2 * D, :]), (w_dst0[D:D + 1, :], ins["be1"][None, :]),
                    (w_edge[0:D, :], we1[2 * D:3 * D, :]), (w_edge[D:P, :], we1[0:D, :]),
                    (w_e2[:, :], ins["We2"]), (w_n1[:, 0, :], ins["Wn1"][0:D, :]),
                    (w_n1[:, 1, :], ins["Wn1"][D:2 * D, :]), (w_n2[:, :], ins["Wn2"]),
                    (bn1[:, :], ins["bn1"][:, None]), (w_1[0:D, 0:D], w1[D:2 * D, :]),
                    (w_1a[0:D, :], w1[0:D, :]), (w_1a[D:D + 1, :], ins["b1"][None, :]),
                    (w_2[:, :], ins["W2"]), (b2[:, :], ins["b2"][:, None]),
                    (be2[:, :], ins["be2"].partition_broadcast(P)),
                    (bn2[:, :], ins["bn2"].partition_broadcast(P))):
                sp.dma_start(dst, src).then_inc(s_w, 16)
            sp.wait_ge(s_ep, 1)
            sp.dma_start(dst_f.rearrange("a b -> (a b)").rearrange("(p w) -> p w", p=ITERS), prep["df"]).then_inc(s_dstf, 16)
            sp.dma_start(prep["dm"], dst_ext[0, 0:EDGES].rearrange("(p w) -> p w", p=ITERS)).then_inc(s_dst, 16)
            sp.wait_ge(s_ep, 7)
            sp.dma_start(base_d[0].rearrange("(p w) -> p w", p=ITERS), prep["base"]).then_inc(s_base, 16)
            sp.wait_ge(s_base, 16)
            sp.dma_start(tile_base[:, :], base_d).then_inc(s_base_in, 16)
            sp.dma_start(xn[:, :, :], x_rows.rearrange("(p c) d -> p c d", p=P)).then_inc(s_x, 16)
            sp.wait_ge(s_base_in, 16)
            sp.wait_ge(s_zero, 1)
            _, past = nc.values_load_multi_w_load_instructions(
                tile_base[0:1, ETILES - TILES:ETILES], engines=(mybir.EngineType.SP,), min_val=0, max_val=RANKS - P)
            for tab, width in zip(rank_tab, (H, D)):
                sp.dma_start(tab[bass.ds(past[TILES - 1], P), :], zeros[:, 0:width]).then_inc(s_fill, 16)
            sp.wait_ge(s_fill, 32)

            for n, ring in enumerate(passes):
                width = (H, D)[n]
                for k in range(2):
                    sp.wait_ge((s_pscat, sweeps[0].scattered)[n][k], CHUNK_DMAS * CHUNKS // 2)
                if n == 1:
                    sp.wait_ge(sweeps[0].kept, CHUNKS)

                def body(it, n=n, ring=ring, width=width):
                    _, base = nc.values_load_multi_w_load_instructions(
                        tile_base[0:1, bass.ds(it * BTILES, BTILES)], engines=(mybir.EngineType.SP,),
                        min_val=0, max_val=RANKS - P)
                    for j in range(RING):
                        g = Step(RING, it, j)
                        hold(sp, ring.pre, g.n - (RING - 1))
                        for t in range(TILES):
                            sp.dma_start(main["win"][:, j, t, 0:width],
                                         rank_tab[n][bass.ds(base[j * TILES + t], P), :]).then_inc(ring.windows[j], 16)

                body(0)
                with sp.Fori(1, ITERS) as it:
                    body(it)

            for k in range(2):
                sp.wait_ge(sweeps[1].stored[k], 16 * CHUNKS // 2)

        @block.gpsimd
        def _(pool):
            def gather(n, g):
                ring = passes[n]
                if n == 0:
                    hold(pool, ring.idx, g.n + 1 - RING)
                else:
                    hold(pool, ring.idx, g.n + 1)
                for t in range(TILES):
                    pool.indirect_dma_start(rows_in[:, g.slot, t, :], None, (x_rows, src_tab1)[n],
                                            bass.IndirectOffsetOnAxis(eidx[:, g.slot, t:t + 1].bitcast(U32), 0)
                                            ).then_inc(ring.gathered[g.slot], 16)

            def scatter(table, rows, k, s):
                width = table.shape[1]
                for c in range(CCOL):
                    pool.indirect_dma_start(table, bass.IndirectOffsetOnAxis(sidx[:, k, c:c + 1].bitcast(U32), 0),
                                            rows[:, k, c * width:(c + 1) * width], None,
                                            bounds_check=RANKS - 1, oob_is_err=False).then_inc(s[k], 16)

            pool.iota(node_i[:, :], [[1, COLS]], base=0, channel_multiplier=COLS)
            pool.iota(part_i[:, :], [[0, 1]], base=0, channel_multiplier=1)
            pool.memset(zeros[:, :], 0.0).then_inc(s_zero, 1)
            pool.memset(ident[:, :], 0.0)
            pool.memset(tri[:, :], 1.0)
            pool.memset(shift[:, :], 0.0)
            pool.memset(eps[:, :], EPS).then_inc(s_zero, 1)
            pool.wait_ge(s_zero, 2)
            pool.affine_select(ident[:, :], ident[:, :], [[-1, P]], ALU.not_equal, 1.0, base=0, channel_multiplier=1)
            pool.affine_select(tri[:, :], tri[:, :], [[1, P]], ALU.is_gt, 0.0, base=0, channel_multiplier=-1)
            pool.affine_select(shift[:, :], shift[:, :], [[1, P]], ALU.not_equal, 1.0, base=-1, channel_multiplier=-1).then_inc(s_const, 1)

            pool.wait_ge(s_first, 16)
            for j in range(RING):
                gather(0, Step(RING, 0, j))

            pool.wait_ge(s_dstf, 16)

            def fetch_row(c):
                hold(pool, s_sidx, c.n + 1)
                for col in range(CCOL):
                    pool.indirect_dma_start(prep["rows"][:, c.slot, col, :], None, dst_f,
                                            bass.IndirectOffsetOnAxis(gidx[:, c.slot, col:col + 1].bitcast(U32), 0)
                                            ).then_inc(s_srow[c.slot], 16)
            run_pipeline(pool, 2, CHUNKS, [(0, fetch_row)])


            def scatter_pre(c):
                hold(pool, s_pcopy, c.n + 1)
                scatter(rank_tab[0], pre_rows, c.slot, s_pscat)
            run_pipeline(pool, 2, CHUNKS, [(0, scatter_pre)])

            def sweep(n):
                ring = sweeps[n]
                for k in range(RING):
                    pool.wait_ge(passes[n].stored[k], 16 * ITERS)

                def fetch(c):
                    hold(pool, ring.idx, c.n + 1)
                    for col in range(CCOL):
                        pool.indirect_dma_start(swp["got"][:, c.slot, col, :], None, edge_rows[n],
                                                bass.IndirectOffsetOnAxis(gidx[:, c.slot, col:col + 1].bitcast(U32), 0)
                                                ).then_inc(ring.got[c.slot], 16)

                def scatter_dst(c):
                    hold(pool, ring.tab, c.n + 1)
                    scatter(rank_tab[1], swp["at"], c.slot, ring.scattered)

                run_pipeline(pool, 2, CHUNKS, [(0, fetch), (X1T_LAG + 2, scatter_dst)] if n == 0 else [(0, fetch)])

            run_pipeline(pool, RING, GROUPS, [(0, lambda g: gather(0, g))], first=RING)
            sweep(0)
            for k in range(2):
                pool.wait_ge(sweeps[0].stored[k], 16 * CHUNKS // 2)
            run_pipeline(pool, RING, GROUPS, [(0, lambda g: gather(1, g))])
            sweep(1)

        @block.tensor
        def _(pe):
            pe.wait_ge(s_const, 1)
            pe.wait_ge(s_w, 256)
            pe.wait_ge(s_ones, 2)

            def pre_products(c):
                wait(pe, s_pcopy, c.n - 1)
                pe.wait_ge(s_xc[c.slot], 16 * c.turn + 16)
                for col in range(CCOL):
                    last = pe.matmul(ps[:, 3 + 2 * c.slot + col // 4, (col % 4) * P:(col % 4 + 1) * P],
                                     xchunk[:, c.slot, col * P:(col + 1) * P], w_dst0[:, :], start=True, stop=True)
                last.then_inc(s_ppre, 1)
            for k in range(2):
                pre_products(Step(2, 0, k))
            pe.wait_ge(s_np, 1)
            pe.matmul(ps[:, 1, 0:1], shift[:, :], cum[:, COLS - 1:COLS], start=True, stop=True).then_inc(s_noff, 1)
            pe.wait_ge(s_np, 6)
            pe.matmul(ps[:, 2, 0:1], tri[:, :], rank[:, COLS - 1:COLS], start=True, stop=True).then_inc(s_noff, 1)
            pe.wait_ge(s_ep, 3)
            pe.matmul(ps[0:ITERS, 0, 0:1], tri[0:ITERS, 0:ITERS], prep["count"][:, BODY - 1:BODY], start=True, stop=True).then_inc(s_off, 1)
            run_pipeline(pe, 2, CHUNKS, [(0, pre_products)], first=2)

            def edge_pass(n):
                ring = passes[n]
                xt_ps, rank_ps, mask_ps, h_ps = ps[:, 0, :], ps[:, 1, :], ps[:, 2:4, :], ps[:, 4:6, :]
                M = (H, D)[n]

                def spread(row, dst, g):
                    return pe.matmul(dst, ident_b[0:ITERS, bass.ds(g.turn, 1)].broadcast_to([ITERS, P]),
                                     marks[:, row, g.slot * GROUP:(g.slot + 1) * GROUP], start=True, stop=True)

                def ranks(g):
                    wait(pe, ring.onehot, g.n)
                    spread(RANK_IN_TILE, rank_ps, g).then_inc(ring.ranks, 1)

                def mask(g):
                    wait(pe, ring.scan, g.n - 1)
                    spread((SAME, PENALTY)[n], mask_ps[:, g.pair, :], g).then_inc(ring.mask, 1)

                def turn(g):
                    pe.wait_ge(ring.gathered[g.slot], 16 * TILES * g.turn + 16 * TILES)
                    hold(pe, ring.stacked, g.n)
                    for t in range(TILES):
                        last = pe.transpose(xt_ps[0:D, t * P:(t + 1) * P], rows_in[:, g.slot, t, :], ident[:, :])
                    last.then_inc(ring.turned, 1)

                def hidden(g):
                    wait(pe, ring.hid, g.n - 1)
                    if n == 0:
                        pe.wait_ge(ring.edges[g.slot], 16 * g.turn + 16)
                        pe.wait_ge(ring.stacked, g.n + 1)
                        pe.matmul(h_ps[:, g.pair, :], w_edge[:, :], main["stack"][:, g.slot, :], start=True, stop=False)
                    else:
                        pe.wait_ge(ring.gathered[g.slot], 16 * TILES * g.turn + 16 * TILES)
                    pe.wait_ge(ring.windows[g.slot], 16 * TILES * g.turn + 16 * TILES)
                    pe.wait_ge(ring.onehot, g.n + 1)
                    for t in range(TILES):
                        o = h_ps[0:M, g.pair, t * P:(t + 1) * P]
                        if n == 1:
                            pe.matmul(o, rows_in[:, g.slot, t, :], ident[:, :], start=True, stop=False)
                        last = pe.matmul(o, main["win"][:, g.slot, t, 0:M], main["onehot"][:, g.pair, t * P:(t + 1) * P],
                                         start=False, stop=(n == 1 or t == TILES - 1))
                    last.then_inc(ring.pre, 1)

                def message(g):
                    pe.wait_ge(ring.hid, g.n + 1)
                    hold(pe, ring.msg, g.n - 1)
                    pe.matmul(ps[0:D, 7 * g.pair, :], w_2[:, :], main["hid"][0:D, g.pair, :],
                              start=True, stop=True).then_inc(ring.msgp, 1)

                def rows(g):
                    pe.wait_ge(ring.scan, g.n + 1)
                    hold(pe, ring.rows, g.n - (1 - n))
                    for t in range(TILES):
                        if n == 0:
                            last = pe.matmul(ps[:, 6 + g.pair, t * D:(t + 1) * D],
                                             main["scan"][:, g.slot, t:GROUP:TILES], w_e2[:, :], start=True, stop=True)
                        else:
                            last = pe.transpose(ps[:, 6, t * D:(t + 1) * D], main["scan"][0:D, g.slot, t:GROUP:TILES], ident[0:D, 0:D])
                    last.then_inc(ring.rowsp, 1)

                if n == 0:
                    run_pipeline(pe, RING, GROUPS, [(0, ranks), (0, turn), (1, mask), (3, rows), (1, hidden)])
                else:
                    run_pipeline(pe, RING, GROUPS, [(0, ranks), (4, rows), (2, mask), (2, message), (1, hidden)])

            def node_sweep():
                ring = sweeps[0]

                def banks01(b):
                    return ps[0:D, b // 4, (b % 4) * P:(b % 4 + 1) * P]

                def turn_agg(c):
                    pe.wait_ge(ring.agg, c.n + 1)
                    hold(pe, ring.x1t, c.n - (X1T_LAG - AGG_LAG))
                    for col in range(CCOL):
                        last = pe.transpose(banks01(col), swp["agg"][:, col, :], ident[:, :])
                    last.then_inc(ring.aggp, 1)

                def hidden(c):
                    pe.wait_ge(ring.x[c.slot], 16 * c.turn + 16)
                    pe.wait_ge(ring.aggt, c.n + 1)
                    wait(pe, ring.h2, c.n)
                    for b, (lo, hi) in enumerate(HALVES):
                        w = (hi - lo) * P
                        pe.matmul(ps[:, 2 + b, 0:w], w_n1[:, 0, :], swp["aggt"][:, lo * P:hi * P], start=True, stop=False)
                        last = pe.matmul(ps[:, 2 + b, 0:w], w_n1[:, 1, :], xchunk[0:D, c.slot, lo * P:hi * P],
                                         start=False, stop=True)
                    last.then_inc(ring.h2p, 1)

                def new_nodes(c):
                    pe.wait_ge(ring.h2, c.n + 1)
                    wait(pe, ring.newr, c.n)
                    for col in range(CCOL):
                        last = pe.matmul(ps[:, 4, col * D:(col + 1) * D], swp["h2"][:, col * P:(col + 1) * P], w_n2[:, :],
                                         start=True, stop=True)
                    last.then_inc(ring.newp, 1)

                def turn_x1(c):
                    pe.wait_ge(ring.x1, c.n + 1)
                    ahead = c.n + (X1T_LAG - AGG_LAG) + 1
                    if isinstance(c.n, int):
                        pe.wait_ge(ring.aggt, min(ahead, CHUNKS))
                    else:
                        hold(pe, ring.aggt, ahead)
                    for col in range(CCOL):
                        last = pe.transpose(banks01(col), swp["x1"][:, c.slot, col, :], ident[:, :])
                    last.then_inc(ring.x1p, 1)

                def tables(c):
                    pe.wait_ge(ring.x1t, c.n + 1)
                    wait(pe, ring.tab, c.n)
                    for col in range(CCOL):
                        last = pe.matmul(ps[:, 5 + col // 4, (col % 4) * P:(col % 4 + 1) * P],
                                         swp["x1t"][:, col * P:(col + 1) * P], w_1[:, :], start=True, stop=True)
                    last.then_inc(ring.tabp, 1)
                run_pipeline(pe, 2, CHUNKS, [(AGG_LAG, turn_agg), (X1T_LAG + 1, tables), (X1T_LAG, turn_x1),
                                             (AGG_LAG + 1, new_nodes), (AGG_LAG, hidden)])

            pe.wait_ge(s_ep, 7)
            edge_pass(0)
            pe.wait_ge(s_w1, 1)
            node_sweep()
            edge_pass(1)

        @block.scalar
        def _(act):
            def load_x(c, s, used):
                wait(act, used, c.n - 1)
                act.dma_start(xchunk[0:D, c.slot, :], x_cols[:, bass.ds(c.n * CW, CW)]).then_inc(s[c.slot], 16)

            def pre_out(c):
                act.wait_ge(s_ppre, c.n + 1)
                wait(act, s_pscat[c.slot], CHUNK_DMAS * c.turn)
                act.copy(pre_rows[:, c.slot, 0:4 * P], ps[:, 3 + 2 * c.slot, :])
                act.copy(pre_rows[:, c.slot, 4 * P:CW], ps[:, 4 + 2 * c.slot, 0:CW - 4 * P])
                if isinstance(c.n, int) and c.n < 2:
                    act.wait_ge(s_np, 9)
                act.copy(sidx[:, c.slot, :], rank_idx[:, chunk_cols(c)]).then_inc(s_pcopy, 1)
            act.wait_ge(s_small, 4)

            def by_rows(c):
                for col in range(CCOL - VCOL):
                    m = c.n * (CCOL - VCOL) + col
                    wait(act, s_signs, m - 1)
                    at = bass.ds(c.n * CCOL + VCOL + col, 1)
                    act.activation(prep["junk_s"][:, (c.slot * (CCOL - VCOL) + col) % 2, :], prep["last_f"], ACT.Sign,
                                   bias=node_h[:, at], scale=-1.0, accum_out=signs[:, at]).then_inc(s_signs, 1)
            run_pipeline(act, 2, CHUNKS, [(0, by_rows)])
            run_pipeline(act, 2, CHUNKS, [(0, lambda c: load_x(c, s_xc, s_ppre)), (1, pre_out)])

            def edge_pass(n):
                ring = passes[n]
                M = (H, D)[n]
                for k in range(2):
                    act.wait_ge((s_pscat, sweeps[0].scattered)[n][k], CHUNK_DMAS * CHUNKS // 2)

                def edges(g):
                    wait(act, ring.pre, g.n - (RING - 1))
                    act.dma_start(main["stack"][D:P, g.slot, :], edges_t[:, bass.ds(g.n * GROUP, GROUP)]).then_inc(ring.edges[g.slot], 16)

                def stack(g):
                    act.wait_ge(ring.turned, g.n + 1)
                    wait(act, ring.pre, g.n - (RING - 1))
                    act.copy(main["stack"][0:D, g.slot, :], ps[0:D, 0, :]).then_inc(ring.stacked, 1)

                def relu(g):
                    act.wait_ge(ring.pre, g.n + 1)
                    wait(act, ring.scan if n == 0 else ring.msgp, g.n - 1)
                    act.activation(main["hid"][0:M, g.pair, :], ps[0:M, 4 + g.pair, :], ACT.Relu).then_inc(ring.hid, 1)

                def message(g):
                    act.wait_ge(ring.msgp, g.n + 1)
                    wait(act, ring.scan, g.n - 1)
                    act.activation(main["msg"][0:D, g.pair, :], ps[0:D, 7 * g.pair, :], ACT.Identity,
                                   bias=b2[:, 0:1]).then_inc(ring.msg, 1)

                def rows(g):
                    act.wait_ge(ring.rowsp, g.n + 1)
                    wait(act, ring.stored[g.slot], 16 * g.turn)
                    act.copy(main["orow"][:, g.slot, :], ps[:, 6 + (1 - n) * g.pair, 0:TILES * D]).then_inc(ring.rows, 1)

                def store(g):
                    act.wait_ge(ring.rows, g.n + 1)
                    act.dma_start(edge_rows[n][bass.ds(g.n * GROUP, GROUP), :].rearrange("(p t) d -> p (t d)", p=P),
                                  main["orow"][:, g.slot, :]).then_inc(ring.stored[g.slot], 16)

                if n == 0:
                    run_pipeline(act, RING, GROUPS, [(0, edges), (2, stack), (5, rows), (3, relu), (6, store)])
                else:
                    run_pipeline(act, RING, GROUPS, [(4, rows), (2, message), (1, relu), (5, store)])

            def node_sweep(n):
                ring = sweeps[n]

                def deviation(c):
                    act.wait_ge(ring.var, c.n + 1)
                    act.activation(swp["std"], swp["var"], ACT.Sqrt, bias=eps[:, 0:1], scale=1.0 / D).then_inc(ring.std, 1)

                def agg_out(c):
                    act.wait_ge(ring.aggp, c.n + 1)
                    wait(act, ring.h2p, c.n)
                    act.copy(swp["aggt"][:, 0:4 * P], ps[0:D, 0, :])
                    act.copy(swp["aggt"][:, 4 * P:], ps[0:D, 1, 0:CW - 4 * P]).then_inc(ring.aggt, 1)

                def relu(c):
                    act.wait_ge(ring.h2p, c.n + 1)
                    wait(act, ring.newp, c.n)
                    act.activation(swp["h2"][:, 0:4 * P], ps[:, 2, :], ACT.Relu, bias=bn1[:, 0:1])
                    act.activation(swp["h2"][:, 4 * P:], ps[:, 3, 0:CW - 4 * P], ACT.Relu,
                                   bias=bn1[:, 0:1]).then_inc(ring.h2, 1)

                def x1_out(c):
                    act.wait_ge(ring.x1p, c.n + 1)
                    wait(act, ring.tabp, c.n)
                    act.copy(swp["x1t"][0:D, 0:4 * P], ps[0:D, 0, :])
                    act.copy(swp["x1t"][0:D, 4 * P:], ps[0:D, 1, 0:CW - 4 * P]).then_inc(ring.x1t, 1)
                    act.copy(xn[:, chunk_cols(c), :], swp["x1"][:, c.slot, :, :]).then_inc(ring.kept, 1)

                def tables_out(c):
                    act.wait_ge(ring.tabp, c.n + 1)
                    wait(act, ring.stored[c.slot], 16 * c.turn)
                    wait(act, ring.scattered[c.slot], CHUNK_DMAS * c.turn)
                    for b, (lo, hi) in enumerate(HALVES):
                        v = ps[:, 5 + b, 0:(hi - lo) * P].rearrange("p (c f) -> p c f", f=P)
                        act.copy(swp["bt"][:, c.slot, lo:hi, :], v[:, :, 0:D])
                        act.copy(swp["at"][:, c.slot, lo * D:hi * D].rearrange("p (c d) -> p c d", d=D), v[:, :, D:P])
                    act.copy(sidx[:, c.slot, :], rank_idx[:, chunk_cols(c)]).then_inc(ring.tab, 1)

                def store_src(c):
                    act.wait_ge(ring.tab, c.n + 1)
                    act.dma_start(src_tab1.rearrange("(p c) d -> p c d", p=P)[:, chunk_cols(c), :],
                                  swp["bt"][:, c.slot, :, :]).then_inc(ring.stored[c.slot], 16)

                def store(c):
                    act.wait_ge(ring.x1, c.n + 1)
                    act.dma_start(out.rearrange("(p c) d -> p (c d)", p=P)[:, bass.ds(c.n * CCOL * D, CCOL * D)],
                                  swp["res"][:, c.slot, :]).then_inc(ring.stored[c.slot], 16)

                if n == 0:
                    act.wait_ge(s_ppre, CHUNKS)
                    for k in range(RING):
                        act.wait_ge(passes[0].stored[k], 16 * ITERS)
                    run_pipeline(act, 2, CHUNKS, [
                        (0, lambda c: load_x(c, ring.x, ring.h2p)), (AGG_LAG, agg_out), (3, deviation),
                        (X1T_LAG, x1_out), (X1T_LAG + 1, tables_out), (X1T_LAG + 1, store_src), (AGG_LAG, relu)])
                else:
                    def prefill(c):
                        wait(act, ring.v, c.n * LINKS[1])
                        act.copy(swp["y"], xn[:, chunk_cols(c), :]).then_inc(ring.copied, 1)
                    for k in range(RING):
                        act.wait_ge(passes[1].stored[k], 16 * ITERS)
                    run_pipeline(act, 2, CHUNKS, [(0, prefill), (0, deviation), (0, store)])

            edge_pass(0)
            node_sweep(0)
            edge_pass(1)
            node_sweep(1)

        @block.vector
        def _(dve):
            dve.memset(xchunk[D:D + 1, :, :], 1.0).then_inc(s_ones, 1)
            dve.wait_ge(s_dst, 16)
            dve.tensor_copy(prep["df"], prep["d0"]).then_inc(s_ep, 1)
            dve.wait_ge(s_last, 16)
            dve.tensor_copy(prep["last_f"], prep["last_i"]).then_inc(s_small, 1)
            dve.wait_ge(s_const, 1)
            dve.tensor_copy(node[:, :], node_i[:, :]).then_inc(s_small, 1)
            dve.tensor_scalar(node_h[:, :], node_i[:, :], 0.5, None, ALU.add).then_inc(s_small, 1)
            dve.tensor_copy(part[:, :], part_i[:, :]).then_inc(s_small, 1)
            dve.tensor_copy(ident_b[:, :], ident[:, :]).then_inc(s_ones, 1)
            dve.wait_ge(s_small, 4)

            def by_rows(c):
                for col in range(VCOL):
                    wait(dve, s_coarse, c.n * VCOL + col - 1)
                    dve.tensor_scalar(prep["junk"][:, (c.slot * VCOL + col) % 2, :], prep["last_f"],
                                      node[:, bass.ds(c.n * CCOL + col, 1)], None, ALU.is_le, ALU.add,
                                      accum_out=cnt_row[:, bass.ds(c.n * CCOL + col, 1)]).then_inc(s_coarse, 1)

            def row_indices(c):
                wait(dve, s_counted, c.n - 1)
                wait(dve, s_signs, (c.n + 1) * (CCOL - VCOL))
                mine = bass.ds(c.n * CCOL + VCOL, CCOL - VCOL)
                dve.tensor_scalar(cnt_row[:, mine], signs[:, mine], float(EROWS), 0.5, ALU.add, ALU.mult).then_inc(s_joined, 1)
                wait(dve, s_coarse, c.n * VCOL + VCOL)
                hold(dve, s_joined, c.n + 1)
                dve.tensor_copy(gidx[:, c.slot, :], cnt_row[:, chunk_cols(c)]).then_inc(s_sidx, 1)

            def in_row(c):
                dve.wait_ge(s_srow[c.slot], CHUNK_DMAS * c.turn + CHUNK_DMAS)
                for col in range(CCOL):
                    v = prep["rows"][:, c.slot, col, :]
                    last = dve.tensor_scalar(v, v, node[:, bass.ds(c.n * CCOL + col, 1)], None, ALU.is_le, ALU.add,
                                             accum_out=cnt_in[:, bass.ds(c.n * CCOL + col, 1)])
                last.then_inc(s_counted, 1)
            run_pipeline(dve, 2, CHUNKS, [(0, by_rows), (4, in_row), (2, row_indices)])
            dve.wait_ge(s_counted, CHUNKS)

            dve.scalar_tensor_tensor(out=cum[:, :], in0=cnt_row[:, :], scalar=float(EROW), in1=cnt_in[:, :],
                                     op0=ALU.mult, op1=ALU.add).then_inc(s_np, 1)
            dve.wait_ge(s_np, 1)
            dve.tensor_tensor(deg[:, 1:COLS], cum[:, 1:COLS], cum[:, 0:COLS - 1], ALU.subtract).then_inc(s_np, 1)
            dve.wait_ge(s_noff, 1)
            dve.tensor_tensor(deg[:, 0:1], cum[:, 0:1], ps[:, 1, 0:1], ALU.subtract).then_inc(s_np, 1)
            dve.tensor_scalar(end_idx[:, :], cum[:, :], -1.0, 0.0, ALU.add, ALU.max).then_inc(s_np, 1)
            dve.wait_ge(s_np, 4)
            dve.tensor_scalar(has[:, :], deg[:, :], 0.0, None, ALU.is_gt).then_inc(s_np, 1)
            dve.wait_ge(s_np, 5)
            dve.tensor_tensor_scan(rank[:, :], has[:, :], has[:, :], 0.0, ALU.add, ALU.max).then_inc(s_np, 1)
            dve.wait_ge(s_noff, 2)
            dve.tensor_scalar(rank_a[:, :], rank[:, :], ps[:, 2, 0:1], -1.0 - SKIP, ALU.add, ALU.add).then_inc(s_np, 1)
            dve.wait_ge(s_np, 7)
            dve.tensor_tensor(rank_b[:, :], rank_a[:, :], has[:, :], ALU.mult).then_inc(s_np, 1)
            dve.wait_ge(s_np, 8)
            dve.tensor_scalar(rank_idx[:, :], rank_b[:, :], float(SKIP), None, ALU.add).then_inc(s_np, 1)

            dve.wait_ge(s_dst, 32)
            dve.tensor_tensor(prep["first"], prep["d0"], prep["dm"], ALU.not_equal).then_inc(s_ep, 1)
            dve.wait_ge(s_ep, 2)
            dve.tensor_tensor_scan(prep["count"], prep["first"], prep["first"], 0.0, ALU.add, ALU.max).then_inc(s_ep, 1)
            dve.tensor_scalar(marks[:, SAME, :], prep["first"], -1.0, 1.0, ALU.mult, ALU.add).then_inc(s_ep, 1)
            dve.tensor_scalar(marks[:, PENALTY, :], prep["first"], -BIG, None, ALU.mult).then_inc(s_ep, 1)
            dve.wait_ge(s_ep, 5)
            tiles = prep["count"].rearrange("p (t e) -> p t e", e=P)
            dve.tensor_tensor(marks[:, RANK_IN_TILE, :].rearrange("p (t e) -> p t e", e=P), tiles,
                              tiles[:, :, 0:1].broadcast_to([ITERS, BTILES, P]), ALU.subtract).then_inc(s_ep, 1)
            dve.wait_ge(s_off, 1)
            dve.tensor_scalar(prep["base"], tiles[:, :, 0], ps[0:ITERS, 0, 0:1], -1.0, ALU.add, ALU.add).then_inc(s_ep, 1)
            dve.tensor_scalar(lacks[:, :], has[:, :], -1.0, 1.0, ALU.mult, ALU.add)

            dve.wait_ge(s_w, 256)
            dve.tensor_tensor(w_1[0:D, D:2 * D], w_1a[0:D, :], w_1[0:D, 0:D], ALU.subtract)
            dve.memset(w_1[D:D + 1, 0:D], 0.0)
            dve.tensor_copy(w_1[D:D + 1, D:2 * D], w_1a[D:D + 1, :]).then_inc(s_w1, 1)
            dve.wait_ge(s_x, 16)
            dve.tensor_tensor(xn[:, :, :], xn[:, :, :],
                              bn2[:, :].rearrange("p (o d) -> p o d", o=1).broadcast_to([P, COLS, D]), ALU.add).then_inc(s_w1, 1)

            def edge_pass(n):
                ring = passes[n]
                M = (H, D)[n]

                def indices(g):
                    hold(dve, ring.turned if n == 0 else ring.pre, g.n + 1)
                    dve.tensor_copy(eidx[:, g.slot, :], esrc[:, bass.ds((g.n + RING) * TILES, TILES)]).then_inc(ring.idx, 1)

                def onehot(g):
                    dve.wait_ge(ring.ranks, g.n + 1)
                    wait(dve, ring.pre, g.n - 1)
                    dve.tensor_scalar(main["onehot"][:, g.pair, :], ps[:, 1, :], part[:, 0:1], None,
                                      ALU.is_equal).then_inc(ring.onehot, 1)

                def scan(g):
                    dve.wait_ge(ring.hid if n == 0 else ring.msg, g.n + 1)
                    dve.wait_ge(ring.mask, g.n + 1)
                    wait(dve, ring.rowsp, g.n - (RING - 1))
                    wait(dve, ring.scan, g.n)
                    before = (g.slot - 1) % RING
                    data = main["hid"] if n == 0 else main["msg"]
                    ops = (ALU.mult, ALU.add) if n == 0 else (ALU.add, ALU.max)
                    dve.tensor_tensor_scan(main["scan"][0:M, g.slot, :], ps[0:M, 2 + g.pair, :], data[0:M, g.pair, :],
                                           main["scan"][0:M, before, GROUP - 1:GROUP], *ops).then_inc(ring.scan, 1)

                if n == 0:
                    for k in range(2):
                        dve.wait_ge(s_pscat[k], CHUNK_DMAS * CHUNKS // 2)
                    dve.wait_ge(s_base, 16)
                    dve.wait_ge(s_dstf, 16)
                    dve.wait_ge(s_src, 16)
                else:
                    dve.wait_ge(sweeps[0].kept, CHUNKS)
                    for k in range(2):
                        dve.wait_ge(sweeps[0].scattered[k], CHUNK_DMAS * CHUNKS // 2)
                        dve.wait_ge(sweeps[0].stored[k], 16 * CHUNKS // 2)
                    for j in range(RING):
                        dve.tensor_copy(eidx[:, j, :], esrc[:, j * TILES:(j + 1) * TILES]).then_inc(ring.idx, 1)
                dve.memset(main["scan"][0:M, RING - 1, GROUP - 1:GROUP], 0.0).then_inc(s_carry, 1)
                dve.wait_ge(s_carry, 1 + n)
                run_pipeline(dve, RING, GROUPS, [(2 + n, scan), (0, onehot), (n, indices)])

            def node_sweep(n):
                ring = sweeps[n]
                wide = [P, CCOL, D]

                def per_node(v):
                    return v.rearrange("p (c o) -> p c o", o=1).broadcast_to(wide)

                def per_feature(v):
                    return v.rearrange("p (o d) -> p o d", o=1).broadcast_to(wide)

                def indices(c):
                    hold(dve, ring.agg if n == 0 else ring.x1, c.n - 1)
                    dve.tensor_copy(gidx[:, c.slot, :], end_idx[:, chunk_cols(c)]).then_inc(ring.idx, 1)

                def aggregate(c):
                    dve.wait_ge(ring.got[c.slot], CHUNK_DMAS * c.turn + CHUNK_DMAS)
                    wait(dve, ring.aggp, c.n)
                    dve.tensor_tensor(swp["agg"], swp["got"][:, c.slot, :, :], per_node(has[:, chunk_cols(c)]), ALU.mult)
                    dve.tensor_tensor(swp["tmp"], per_feature(be2[:, :]), per_node(deg[:, chunk_cols(c)]), ALU.mult).then_inc(ring.a, 1)
                    hold(dve, ring.a, c.n + 1)
                    dve.tensor_tensor(swp["agg"], swp["agg"], swp["tmp"], ALU.add).then_inc(ring.agg, 1)

                def link(c, k, ins):
                    ins.then_inc(ring.v, 1)
                    wait(dve, ring.v, c.n * LINKS[n] + k)

                def norm(c):
                    first = LINKS[n] - 3
                    link(c, first + 1, dve.tensor_reduce(swp["sum"], swp["y"], AX.X, ALU.add))
                    link(c, first + 2, dve.scalar_tensor_tensor(out=swp["cen"], in0=per_node(swp["sum"]), scalar=-1.0 / D,
                                                                in1=swp["y"], op0=ALU.mult, op1=ALU.add))
                    link(c, first + 3, dve.tensor_tensor(swp["sq"], swp["cen"], swp["cen"], ALU.mult))
                    dve.tensor_reduce(swp["var"], swp["sq"], AX.X, ALU.add).then_inc(ring.var, 1)

                def scale(c, dst):
                    dve.wait_ge(ring.std, c.n + 1)
                    dve.reciprocal(swp["rstd"], swp["std"]).then_inc(ring.rstd, 1)
                    wait(dve, ring.rstd, c.n + 1)
                    dve.tensor_tensor(dst, swp["cen"], per_node(swp["rstd"]), ALU.mult).then_inc(ring.x1, 1)

                def norm0(c):
                    dve.wait_ge(ring.newp, c.n + 1)
                    dve.tensor_tensor(swp["y"], ps[:, 4, 0:CCOL * D].rearrange("p (c d) -> p c d", d=D),
                                      xn[:, chunk_cols(c), :], ALU.add).then_inc(ring.newr, 1)
                    wait(dve, ring.newr, c.n + 1)
                    norm(c)

                def scale0(c):
                    wait(dve, ring.x1p, c.n - 1)
                    wait(dve, ring.kept, c.n - 1)
                    scale(c, swp["x1"][:, c.slot, :, :])

                def all1(c):
                    got = swp["got"][:, c.slot, :, :]
                    dve.wait_ge(ring.got[c.slot], CHUNK_DMAS * c.turn + CHUNK_DMAS)
                    dve.scalar_tensor_tensor(out=swp["ok"], in0=got, scalar=0.0, in1=per_node(lacks[:, chunk_cols(c)]),
                                             op0=ALU.mult, op1=ALU.is_equal)
                    link(c, 1, dve.tensor_tensor(swp["tmp"], got, xn[:, chunk_cols(c), :], ALU.add))
                    hold(dve, ring.copied, c.n + 1)
                    link(c, 2, dve.copy_predicated(swp["y"], swp["ok"], swp["tmp"]))
                    norm(c)
                    wait(dve, ring.stored[c.slot], 16 * c.turn)
                    scale(c, swp["res"][:, c.slot, :].rearrange("p (c d) -> p c d", d=D))

                for k in range(RING):
                    dve.wait_ge(passes[n].stored[k], 16 * ITERS)
                if n == 0:
                    dve.memset(swp["x1t"][D:D + 1, :], 1.0)
                if n == 0:
                    run_pipeline(dve, 2, CHUNKS, [(0, indices), (3, norm0), (AGG_LAG, aggregate), (3, scale0)])
                else:
                    run_pipeline(dve, 2, CHUNKS, [(0, indices), (1, all1)])

            edge_pass(0)
            node_sweep(0)
            edge_pass(1)
            node_sweep(1)


def kernel(**inputs):
    import numpy as np
    import concourse.bacc as bacc
    from concourse.bass_utils import run_bass_kernel_spmd

    x = np.asarray(inputs["x"])
    edges = np.asarray(inputs["edge_attr_64"])
    n_nodes, n_edges = x.shape[0], edges.shape[0]
    cols, iters = sizes(n_nodes, n_edges)
    nodes, padded = cols * P, iters * BODY

    x_rows = np.zeros((nodes, D), x.dtype)
    x_rows[:n_nodes] = x
    x_cols = np.ascontiguousarray(x_rows.reshape(P, cols, D).transpose(2, 1, 0)).reshape(D, nodes)
    edges_t = np.zeros((D, padded), edges.dtype)
    edges_t[:, :n_edges] = edges.T
    dst_ext = np.full((1, 1 + padded), nodes, np.int32)
    dst_ext[0, 0] = -1
    dst_ext[0, 1:1 + n_edges] = inputs["dst"]
    dst_last = np.ascontiguousarray(dst_ext[0, 1:].reshape(-1, EROW)[:, -1])
    src = np.zeros(padded + BODY, np.int32)
    src[:n_edges] = inputs["src"]
    src_idx = np.ascontiguousarray(src.reshape(-1, P).T)

    arrays = {"x_rows": x_rows, "x_cols": x_cols, "src_idx": src_idx, "dst_ext": dst_ext,
              "dst_last": dst_last, "edges_t": edges_t}
    for name in ("We1", "be1", "We2", "be2", "Wn1", "bn1", "Wn2", "bn2"):
        arrays[name] = np.ascontiguousarray(inputs["L0_gnn_" + name])
    for name in ("W1", "b1", "W2", "b2"):
        arrays[name] = np.ascontiguousarray(inputs["L1_gnn_" + name])

    nc = bacc.Bacc("TRN2", target_bir_lowering=False, num_devices=1)
    ins = {k: nc.dram_tensor(k + "_dram", a.shape, mybir.dt.from_np(a.dtype), kind="ExternalInput").ap()
           for k, a in arrays.items()}
    out = nc.dram_tensor("out_dram", (nodes, D), F32, kind="ExternalOutput").ap()
    build(nc, ins, out)
    ran = run_bass_kernel_spmd(nc, [{k + "_dram": a for k, a in arrays.items()}], core_ids=[0])
    return ran.results[0]["out_dram"][:n_nodes]
```
